# Optimizing a Trainium2 kernel written in Bass

```python
import numpy as np
import jax
import jax.numpy as jnp

def _softmax(x, axis=-1):
    return jax.nn.softmax(x, axis=axis)

def _gelu(x):
    return jax.nn.gelu(x, approximate=True)

def _silu(x):
    return jax.nn.silu(x)

def _sigmoid(x):
    return jax.nn.sigmoid(x)

def _layernorm(x, axis=-1, eps=1e-05):
    m = jnp.mean(x, axis=axis, keepdims=True)
    v = jnp.var(x, axis=axis, keepdims=True)
    return (x - m) / jnp.sqrt(v + eps)

def _scatter_add(tgt, idx, src, axis=0):
    return tgt.at[idx].add(src)

def _segment_sum(src, seg, n):
    return jax.ops.segment_sum(src, seg, n)
kernel_name = 'mk_dlrm_tower_d1_rec_r8_85b26d'

def setup_inputs(seed: int=0):
    np.random.seed(seed)
    _w = jnp.asarray

    def _rec_inputs():
        import jax
        import jax.numpy as jnp
        _tk = jax.random.key(seed)
        dense_ctx = jax.random.normal(jax.random.fold_in(_tk, 190), (2048, 16), jnp.float32)
        ids = jnp.stack([jax.random.randint(jax.random.fold_in(_tk, 200 + f), (2048,), 0, v, jnp.int32) for f, v in enumerate([1250, 1250, 12500, 12500, 1000, 1250, 12500, 1000, 1000, 12500, 1250, 1250, 1250, 1000, 1250, 1250, 1000, 1250, 1000, 1250, 1250, 12500, 1250, 12500, 1250, 12500, 1250, 12500, 1250, 1000, 1000, 1000])], axis=1)
        tbl_0 = 0.05 * jax.random.normal(jax.random.fold_in(_tk, 500 + 0), (1250, 256), jnp.float32)
        tbl_1 = 0.05 * jax.random.normal(jax.random.fold_in(_tk, 500 + 1), (1250, 256), jnp.float32)
        tbl_2 = 0.05 * jax.random.normal(jax.random.fold_in(_tk, 500 + 2), (12500, 256), jnp.float32)
        tbl_3 = 0.05 * jax.random.normal(jax.random.fold_in(_tk, 500 + 3), (12500, 256), jnp.float32)
        tbl_4 = 0.05 * jax.random.normal(jax.random.fold_in(_tk, 500 + 4), (1000, 256), jnp.float32)
        tbl_5 = 0.05 * jax.random.normal(jax.random.fold_in(_tk, 500 + 5), (1250, 256), jnp.float32)
        tbl_6 = 0.05 * jax.random.normal(jax.random.fold_in(_tk, 500 + 6), (12500, 256), jnp.float32)
        tbl_7 = 0.05 * jax.random.normal(jax.random.fold_in(_tk, 500 + 7), (1000, 256), jnp.float32)
        tbl_8 = 0.05 * jax.random.normal(jax.random.fold_in(_tk, 500 + 8), (1000, 256), jnp.float32)
        tbl_9 = 0.05 * jax.random.normal(jax.random.fold_in(_tk, 500 + 9), (12500, 256), jnp.float32)
        tbl_10 = 0.05 * jax.random.normal(jax.random.fold_in(_tk, 500 + 10), (1250, 256), jnp.float32)
        tbl_11 = 0.05 * jax.random.normal(jax.random.fold_in(_tk, 500 + 11), (1250, 256), jnp.float32)
        tbl_12 = 0.05 * jax.random.normal(jax.random.fold_in(_tk, 500 + 12), (1250, 256), jnp.float32)
        tbl_13 = 0.05 * jax.random.normal(jax.random.fold_in(_tk, 500 + 13), (1000, 256), jnp.float32)
        tbl_14 = 0.05 * jax.random.normal(jax.random.fold_in(_tk, 500 + 14), (1250, 256), jnp.float32)
        tbl_15 = 0.05 * jax.random.normal(jax.random.fold_in(_tk, 500 + 15), (1250, 256), jnp.float32)
        tbl_16 = 0.05 * jax.random.normal(jax.random.fold_in(_tk, 500 + 16), (1000, 256), jnp.float32)
        tbl_17 = 0.05 * jax.random.normal(jax.random.fold_in(_tk, 500 + 17), (1250, 256), jnp.float32)
        tbl_18 = 0.05 * jax.random.normal(jax.random.fold_in(_tk, 500 + 18), (1000, 256), jnp.float32)
        tbl_19 = 0.05 * jax.random.normal(jax.random.fold_in(_tk, 500 + 19), (1250, 256), jnp.float32)
        tbl_20 = 0.05 * jax.random.normal(jax.random.fold_in(_tk, 500 + 20), (1250, 256), jnp.float32)
        tbl_21 = 0.05 * jax.random.normal(jax.random.fold_in(_tk, 500 + 21), (12500, 256), jnp.float32)
        tbl_22 = 0.05 * jax.random.normal(jax.random.fold_in(_tk, 500 + 22), (1250, 256), jnp.float32)
        tbl_23 = 0.05 * jax.random.normal(jax.random.fold_in(_tk, 500 + 23), (12500, 256), jnp.float32)
        tbl_24 = 0.05 * jax.random.normal(jax.random.fold_in(_tk, 500 + 24), (1250, 256), jnp.float32)
        tbl_25 = 0.05 * jax.random.normal(jax.random.fold_in(_tk, 500 + 25), (12500, 256), jnp.float32)
        tbl_26 = 0.05 * jax.random.normal(jax.random.fold_in(_tk, 500 + 26), (1250, 256), jnp.float32)
        tbl_27 = 0.05 * jax.random.normal(jax.random.fold_in(_tk, 500 + 27), (12500, 256), jnp.float32)
        tbl_28 = 0.05 * jax.random.normal(jax.random.fold_in(_tk, 500 + 28), (1250, 256), jnp.float32)
        tbl_29 = 0.05 * jax.random.normal(jax.random.fold_in(_tk, 500 + 29), (1000, 256), jnp.float32)
        tbl_30 = 0.05 * jax.random.normal(jax.random.fold_in(_tk, 500 + 30), (1000, 256), jnp.float32)
        tbl_31 = 0.05 * jax.random.normal(jax.random.fold_in(_tk, 500 + 31), (1000, 256), jnp.float32)
        _rk = jax.random.fold_in(_tk, 7)
        W_top1 = 0.0441942 * jax.random.normal(jax.random.fold_in(_tk, 801), (512, 512), jnp.float32)
        W_top2 = 0.0441942 * jax.random.normal(jax.random.fold_in(_tk, 802), (512, 256), jnp.float32)
        W_top3 = 0.0625 * jax.random.normal(jax.random.fold_in(_tk, 803), (256, 1), jnp.float32)
        b_top1 = jnp.zeros((512,), jnp.float32)
        b_top2 = jnp.zeros((256,), jnp.float32)
        return (dense_ctx, ids, tbl_0, tbl_1, tbl_2, tbl_3, tbl_4, tbl_5, tbl_6, tbl_7, tbl_8, tbl_9, tbl_10, tbl_11, tbl_12, tbl_13, tbl_14, tbl_15, tbl_16, tbl_17, tbl_18, tbl_19, tbl_20, tbl_21, tbl_22, tbl_23, tbl_24, tbl_25, tbl_26, tbl_27, tbl_28, tbl_29, tbl_30, tbl_31, W_top1, b_top1, W_top2, b_top2, W_top3)
    dense_ctx, ids, tbl_0, tbl_1, tbl_2, tbl_3, tbl_4, tbl_5, tbl_6, tbl_7, tbl_8, tbl_9, tbl_10, tbl_11, tbl_12, tbl_13, tbl_14, tbl_15, tbl_16, tbl_17, tbl_18, tbl_19, tbl_20, tbl_21, tbl_22, tbl_23, tbl_24, tbl_25, tbl_26, tbl_27, tbl_28, tbl_29, tbl_30, tbl_31, W_top1, b_top1, W_top2, b_top2, W_top3 = _rec_inputs()

    def _L0_rec_setup():
        import jax, jax.numpy as jnp
        import numpy as np
        B, N, D = (1024, 32, 256)
        key = jax.random.key(seed)
        x = jax.random.normal(key, (B, N, D), dtype=jnp.float32)
        return {'x': x}
    _L0_rec_all = _L0_rec_setup()
    _L0_rec_in = {k: v for k, v in _L0_rec_all.items() if k in ()}
    del _L0_rec_all
    return {'dense_ctx': dense_ctx, 'ids': ids, 'tbl_0': tbl_0, 'tbl_1': tbl_1, 'tbl_2': tbl_2, 'tbl_3': tbl_3, 'tbl_4': tbl_4, 'tbl_5': tbl_5, 'tbl_6': tbl_6, 'tbl_7': tbl_7, 'tbl_8': tbl_8, 'tbl_9': tbl_9, 'tbl_10': tbl_10, 'tbl_11': tbl_11, 'tbl_12': tbl_12, 'tbl_13': tbl_13, 'tbl_14': tbl_14, 'tbl_15': tbl_15, 'tbl_16': tbl_16, 'tbl_17': tbl_17, 'tbl_18': tbl_18, 'tbl_19': tbl_19, 'tbl_20': tbl_20, 'tbl_21': tbl_21, 'tbl_22': tbl_22, 'tbl_23': tbl_23, 'tbl_24': tbl_24, 'tbl_25': tbl_25, 'tbl_26': tbl_26, 'tbl_27': tbl_27, 'tbl_28': tbl_28, 'tbl_29': tbl_29, 'tbl_30': tbl_30, 'tbl_31': tbl_31, 'W_top1': W_top1, 'b_top1': b_top1, 'W_top2': W_top2, 'b_top2': b_top2, 'W_top3': W_top3}

def reference(dense_ctx, ids, tbl_0, tbl_1, tbl_2, tbl_3, tbl_4, tbl_5, tbl_6, tbl_7, tbl_8, tbl_9, tbl_10, tbl_11, tbl_12, tbl_13, tbl_14, tbl_15, tbl_16, tbl_17, tbl_18, tbl_19, tbl_20, tbl_21, tbl_22, tbl_23, tbl_24, tbl_25, tbl_26, tbl_27, tbl_28, tbl_29, tbl_30, tbl_31, W_top1, b_top1, W_top2, b_top2, W_top3):
    import jax
    import jax.numpy as jnp

    def _L0_rec_ref(x):
        import jax, jax.numpy as jnp
        import numpy as np
        B, N, D = (1024, 32, 256)
        'Second-order feature interaction (DLRM dot interaction).\n\n            Computes dot(x_i, x_j) for all field pairs i < j (self_interaction=False),\n            flattened in row-major upper-triangular order -> [B, N*(N-1)/2].\n            Matches tf.boolean_mask(dot_products, strictly_upper_mask) ordering.\n            '
        b, n, d = x.shape
        iu, ju = jnp.triu_indices(n, k=1)
        dots = jnp.einsum('bnd,bmd->bnm', x, x)
        return dots[:, iu, ju]
    e = jnp.stack([tbl_0[ids[:, 0]], tbl_1[ids[:, 1]], tbl_2[ids[:, 2]], tbl_3[ids[:, 3]], tbl_4[ids[:, 4]], tbl_5[ids[:, 5]], tbl_6[ids[:, 6]], tbl_7[ids[:, 7]], tbl_8[ids[:, 8]], tbl_9[ids[:, 9]], tbl_10[ids[:, 10]], tbl_11[ids[:, 11]], tbl_12[ids[:, 12]], tbl_13[ids[:, 13]], tbl_14[ids[:, 14]], tbl_15[ids[:, 15]], tbl_16[ids[:, 16]], tbl_17[ids[:, 17]], tbl_18[ids[:, 18]], tbl_19[ids[:, 19]], tbl_20[ids[:, 20]], tbl_21[ids[:, 21]], tbl_22[ids[:, 22]], tbl_23[ids[:, 23]], tbl_24[ids[:, 24]], tbl_25[ids[:, 25]], tbl_26[ids[:, 26]], tbl_27[ids[:, 27]], tbl_28[ids[:, 28]], tbl_29[ids[:, 29]], tbl_30[ids[:, 30]], tbl_31[ids[:, 31]]], axis=1)
    z = _L0_rec_ref(e)
    z = z.reshape(z.shape[0], -1)
    h = jnp.concatenate([z, dense_ctx], axis=1)
    h = jnp.maximum(h @ W_top1 + b_top1, 0.0)
    h = jnp.maximum(h @ W_top2 + b_top2, 0.0)
    y = h @ W_top3
    return y

_drawn_inputs = setup_inputs


def setup_inputs(seed=0):
    import zlib

    import numpy as np

    out = dict(_drawn_inputs(seed))
    spreads = {'b_top1': (0.0, 0.1), 'b_top2': (0.0, 0.1)}
    factors = {}
    for name, (base, spread) in spreads.items():
        noise = np.random.default_rng([zlib.crc32(name.encode()), seed]).standard_normal(out[name].shape)
        drawn = base * np.exp(spread * noise) if base else spread * noise
        out[name] = jnp.asarray(drawn.astype(out[name].dtype))
    for name, factor in factors.items():
        out[name] = (out[name] * factor).astype(out[name].dtype)
    return out
```

```python
from contextlib import ExitStack

import concourse.bass as bass
from concourse import mybir

F32 = mybir.dt.float32
I32 = mybir.dt.int32
U32 = mybir.dt.uint32
ALU = mybir.AluOpType
ACT = mybir.ActivationFunctionType

P = 128


def dlrm_tower(nc, dense_t, ids, tables, w1, b1_t, w2, b2_t, w3_t, out):
    NB, NF = ids.shape
    D = tables[0].shape[1]
    ND = dense_t.shape[0]
    H1, H2 = w2.shape
    TILES = NB // P
    HALVES = D // P
    FPS = 4
    SUBS = NF // FPS
    QUADS = P // NF
    GROUPS = P // QUADS
    GPS = GROUPS // SUBS
    BANKG = GROUPS // 2
    KC = NF // QUADS
    M1C, M2C = H1 // P, H2 // P
    assert HALVES == 2 and NF == 32 and TILES % 2 == 0 and BANKG * NF == 512

    with ExitStack() as ctx:
        def sb(name, shape, dt=F32):
            return ctx.enter_context(nc.sbuf_tensor(name, shape, dt))

        def pb(name, shape):
            return ctx.enter_context(nc.psum_tensor(name, shape, F32))

        def sem(name):
            return ctx.enter_context(nc.semaphore(name))

        index = [sb(f"index{p}", [P, NF], U32) for p in range(2)]
        rows = [sb(f"rows{p}", [P, NF, D]) for p in range(2)]
        cols = [sb(f"cols{p}", [P, HALVES, P, NF]) for p in range(2)]
        pairs = [sb(f"pairs{p}", [P, KC, P]) for p in range(2)]
        hidden1 = sb("hidden1", [P, M1C, P])
        hidden2 = sb("hidden2", [P, M2C, P])
        score = [sb(f"score{p}", [P, 1]) for p in range(2)]
        w1_sb = sb("w1_sb", [P, KC, H1])
        w2_sb = sb("w2_sb", [P, M1C, H2])
        w3_sb = sb("w3_sb", [P, M2C])
        b1_sb = sb("b1_sb", [P, M1C])
        b2_sb = sb("b2_sb", [P, M2C])
        identity = sb("identity", [P, P])

        ps_turn = [[pb(f"ps_turn{c}{k}", [P, FPS, P]) for k in range(2)] for c in range(HALVES)]
        ps_gram = [pb(f"ps_gram{h}", [P, BANKG, NF]) for h in range(2)]
        ps_l1 = pb("ps_l1", [P, M1C, P])
        ps_l23 = pb("ps_l23", [P, 512])

        index_loaded = [sem(f"index_loaded{p}") for p in range(2)]
        gathered = [[sem(f"gathered{p}_{u}") for u in range(SUBS)] for p in range(2)]
        transposed = [sem(f"transposed{c}") for c in range(HALVES)]
        cols_ready = [sem(f"cols_ready{c}") for c in range(HALVES)]
        gram_done = [sem(f"gram_done{h}") for h in range(2)]
        pairs_ready = [sem(f"pairs_ready{h}") for h in range(2)]
        dense_loaded = [sem(f"dense_loaded{p}") for p in range(2)]
        l1_done, l2_done, l3_done = sem("l1_done"), sem("l2_done"), sem("l3_done")
        hidden1_ready, hidden2_ready, score_ready = sem("hidden1_ready"), sem("hidden2_ready"), sem("score_ready")
        stored = [sem(f"stored{p}") for p in range(2)]
        gather_started = sem("gather_started")
        identity_zeroed, identity_ready = sem("identity_zeroed"), sem("identity_ready")
        w1_zeroed, pairs_zeroed = sem("w1_zeroed"), sem("pairs_zeroed")
        w1_loaded, w_loaded = sem("w1_loaded"), sem("w_loaded")

        block = ctx.enter_context(nc.Block())

        w1_loads = []
        for i in range(NF):
            first = i * (2 * NF - 1 - i) // 2
            for q in range(QUADS):
                c0 = max(0, i + 1 - KC * q)
                if c0 < KC:
                    w1_loads.append((NF * q + i, c0, first + KC * q + c0 - i - 1, KC - c0))
        N_PAIRS = NF * (NF - 1) // 2
        W1_TOTAL = 16 * (len(w1_loads) + 1)

        out_v = out.rearrange("(t p) o -> t p o", p=P)
        ids_v = ids.rearrange("(t p) f -> t p f", p=P)
        dense_v = dense_t.rearrange("d (t b) -> t d b", b=P)

        @block.sync
        def _(sp):
            def load_index(n, p):
                sp.dma_start(index[p][:, :], ids_v[n].bitcast(U32)).then_inc(index_loaded[p], 16)

            def load_dense(n, p):
                sp.dma_start(pairs[p][0:ND, 0, :], dense_v[n]).then_inc(dense_loaded[p], 16)

            def store(n, p):
                sp.wait_ge(score_ready, n + 1)
                sp.dma_start(out_v[n], score[p][:, :]).then_inc(stored[p], 16)

            load_index(0, 0)
            load_index(1, 1)
            sp.dma_start(b1_sb[:, :], b1_t).then_inc(w_loaded, 16)
            sp.dma_start(b2_sb[:, :], b2_t).then_inc(w_loaded, 16)
            sp.dma_start(w3_sb[:, :], w3_t).then_inc(w_loaded, 16)
            sp.dma_start(w2_sb[:, :, :], w2.rearrange("(m p) n -> p m n", p=P)).then_inc(w_loaded, 16)
            sp.wait_ge(pairs_zeroed, 1)
            load_dense(0, 0)
            load_dense(1, 1)
            sp.wait_ge(w1_zeroed, 1)
            for part, c0, row, n in w1_loads:
                sp.dma_start(w1_sb[part:part + 1, c0:c0 + n, :],
                             w1[row:row + n, :].rearrange("(a c) n -> a c n", a=1)).then_inc(w1_loaded, 16)
            sp.dma_start(w1_sb[0:ND, 0, :], w1[N_PAIRS:N_PAIRS + ND, :]).then_inc(w1_loaded, 16)

            def step(n, p):
                sp.wait_ge(transposed[1], SUBS * (n + 1))
                load_index(n + 2, p)
                sp.wait_ge(l1_done, n + 1)
                load_dense(n + 2, p)
                store(n, p)

            with sp.Fori(0, TILES // 2 - 1) as i:
                step(2 * i, 0)
                step(2 * i + 1, 1)
            store(TILES - 2, 0)
            store(TILES - 1, 1)
            for p in range(2):
                sp.wait_ge(stored[p], 16 * (TILES // 2))

        @block.gpsimd
        def _(pool):
            pool.memset(identity[:, :], 0.0).then_inc(identity_zeroed, 1)

            def gather(p, u, field):
                pool.indirect_dma_start(
                    out=rows[p][:, field, :], out_offset=None, in_=tables[field],
                    in_offset=bass.IndirectOffsetOnAxis(ap=index[p][:, field:field + 1], axis=0),
                ).then_inc(gathered[p][u], 16)

            def gather_tile(n, p):
                pool.wait_ge(index_loaded[p], 8 * (n - p) + 16)
                pool.sem_inc(gather_started, 1)
                for u in range(SUBS):
                    for f in range(FPS):
                        gather(p, u, FPS * u + f)

            gather_tile(0, 0)
            pool.wait_ge(identity_zeroed, 1)
            pool.affine_select(out=identity[:, :], in_=identity[:, :], compare_op=ALU.not_equal, fill=1.0,
                               base=0, pattern=[[-1, P]], channel_multiplier=1).then_inc(identity_ready, 1)
            gather_tile(1, 1)
            with pool.Fori(1, TILES // 2) as i:
                gather_tile(2 * i, 0)
                gather_tile(2 * i + 1, 1)

        @block.tensor
        def _(pe):
            def transposes(n, p, u, fresh=False):
                pe.wait_ge(gathered[p][u], FPS * (8 * (n - p) + 16))
                for c in range(HALVES):
                    if not fresh or u >= 2:
                        pe.wait_ge(cols_ready[c], SUBS * n + u - 1)
                    for f in range(FPS):
                        last = pe.transpose(ps_turn[c][u % 2][:, f, :],
                                            rows[p][:, FPS * u + f, c * P:(c + 1) * P], identity[:, :])
                    last.then_inc(transposed[c], 1)

            def gram(n, p, u, first=False):
                h = u // (SUBS // 2)
                if u == 0:
                    for c in range(HALVES):
                        pe.wait_ge(cols_ready[c], SUBS * (n + 1))
                if u % (SUBS // 2) == 0 and not first:
                    pe.wait_ge(pairs_ready[h], n)
                for g in range(GPS * u, GPS * (u + 1)):
                    for c in range(HALVES):
                        for j in range(QUADS):
                            x = cols[p][:, c, NF * j + g, :]
                            last = pe.matmul(ps_gram[h][NF * j:NF * (j + 1), g % BANKG, :], x, x,
                                             start=(c == 0), stop=(c == HALVES - 1))
                if (u + 1) % (SUBS // 2) == 0:
                    last.then_inc(gram_done[h], 1)

            def layer1(n, p, m, first=False):
                if m == 0:
                    for h in range(2):
                        pe.wait_ge(pairs_ready[h], n + 1)
                    pe.wait_ge(dense_loaded[p], 8 * (n - p) + 16)
                    if first:
                        pe.wait_ge(w1_loaded, W1_TOTAL)
                    else:
                        pe.wait_ge(hidden1_ready, n)
                for c in range(KC):
                    last = pe.matmul(ps_l1[:, m, :], w1_sb[:, c, m * P:(m + 1) * P], pairs[p][:, c, :],
                                     start=(c == 0), stop=(c == KC - 1))
                if m == M1C - 1:
                    last.then_inc(l1_done, 1)

            def layer2(n, first=False):
                pe.wait_ge(hidden1_ready, n + 1)
                if first:
                    pe.wait_ge(w_loaded, 64)
                else:
                    pe.wait_ge(score_ready, n)
                for m in range(M2C):
                    for c in range(M1C):
                        last = pe.matmul(ps_l23[:, m * P:(m + 1) * P], w2_sb[:, c, m * P:(m + 1) * P],
                                         hidden1[:, c, :], start=(c == 0), stop=(c == M1C - 1))
                last.then_inc(l2_done, 1)

            def layer3(n):
                pe.wait_ge(hidden2_ready, n + 1)
                for m in range(M2C):
                    last = pe.matmul(ps_l23[:, H2:H2 + 1], hidden2[:, m, :], w3_sb[:, m:m + 1],
                                     start=(m == 0), stop=(m == M2C - 1))
                last.then_inc(l3_done, 1)

            def step(n, p, turn=True, dots=True, mlp=True, first=False, first_mlp=False):
                for u in range(SUBS):
                    if turn:
                        transposes(n + 1, 1 - p, u)
                    if dots:
                        gram(n, p, u, first)
                    if mlp and 1 <= u <= M1C:
                        layer1(n - 1, 1 - p, u - 1, first_mlp)
                    if mlp and u == M1C + 1:
                        layer2(n - 1, first_mlp)
                    if mlp and u == M1C + 2:
                        layer3(n - 1)

            pe.wait_ge(identity_ready, 1)
            for u in range(SUBS):
                transposes(0, 0, u, fresh=True)
            step(0, 0, mlp=False, first=True)
            step(1, 1, first_mlp=True)
            with pe.Fori(1, TILES // 2 - 1) as i:
                step(2 * i, 0)
                step(2 * i + 1, 1)
            step(TILES - 2, 0)
            step(TILES - 1, 1, turn=False)
            step(TILES, 0, turn=False, dots=False)

        def evacuate(copy, wait, c, n, p, u):
            wait(transposed[c], SUBS * n + u + 1)
            copy(cols[p][:, c, :, FPS * u:FPS * (u + 1)].rearrange("p b f -> p f b"),
                 ps_turn[c][u % 2][:, :, :]).then_inc(cols_ready[c], 1)

        def regroup(copy, wait, h, n, p):
            wait(gram_done[h], n + 1)
            for q in range(QUADS):
                c0 = 1 if q == 0 else 0
                for j in range(QUADS):
                    b = NF * j + BANKG * h
                    last = copy(pairs[p][NF * q:NF * (q + 1), c0:KC, b:b + BANKG].rearrange("p c g -> p g c"),
                                ps_gram[h][NF * j:NF * (j + 1), :, KC * q + c0:KC * (q + 1)])
            last.then_inc(pairs_ready[h], 1)

        @block.scalar
        def _(act):
            def copy(dst, src):
                return act.copy(dst, src)

            def relu1(n, first=False):
                act.wait_ge(l1_done, n + 1)
                if first:
                    act.wait_ge(w_loaded, 64)
                for m in range(M1C):
                    last = act.activation(hidden1[:, m, :], ps_l1[:, m, :], ACT.Relu, bias=b1_sb[:, m:m + 1])
                last.then_inc(hidden1_ready, 1)

            def step(n, p, turn=True, mlp=True, first_mlp=False):
                for u in range(SUBS):
                    if turn:
                        evacuate(copy, act.wait_ge, 0, n + 1, 1 - p, u)
                    if mlp and u == 0:
                        regroup(copy, act.wait_ge, 1, n - 1, 1 - p)
                    if mlp and u == M1C + 1:
                        relu1(n - 1, first_mlp)

            for u in range(SUBS):
                evacuate(copy, act.wait_ge, 0, 0, 0, u)
            act.wait_ge(pairs_zeroed, 1)
            step(0, 0, mlp=False)
            step(1, 1, first_mlp=True)
            with act.Fori(1, TILES // 2 - 1) as i:
                step(2 * i, 0)
                step(2 * i + 1, 1)
            step(TILES - 2, 0)
            step(TILES - 1, 1, turn=False)
            step(TILES, 0, turn=False)

        @block.vector
        def _(dve):
            def copy(dst, src):
                return dve.tensor_copy(dst, src)

            def relu2(n):
                dve.wait_ge(l2_done, n + 1)
                for m in range(M2C):
                    last = dve.tensor_scalar(hidden2[:, m, :], ps_l23[:, m * P:(m + 1) * P], b2_sb[:, m:m + 1],
                                             0.0, ALU.add, ALU.max)
                last.then_inc(hidden2_ready, 1)

            def take_score(n, p, fresh=False):
                dve.wait_ge(l3_done, n + 1)
                if not fresh:
                    dve.wait_ge(stored[p], 8 * (n - p))
                dve.tensor_copy(score[p][:, :], ps_l23[:, H2:H2 + 1]).then_inc(score_ready, 1)

            def step(n, p, turn=True, dots=True, mlp=True, fresh=False):
                for u in range(SUBS):
                    if turn:
                        evacuate(copy, dve.wait_ge, 1, n + 1, 1 - p, u)
                    if dots and u == SUBS // 2:
                        regroup(copy, dve.wait_ge, 0, n, p)
                    if mlp and u == M1C + 2:
                        relu2(n - 1)
                    if mlp and u == M1C + 3:
                        take_score(n - 1, 1 - p, fresh)

            for p in range(2):
                last = dve.memset(pairs[p][0:NF, 0, :], 0.0)
            last.then_inc(pairs_zeroed, 1)
            dve.memset(w1_sb[:, :, :], 0.0).then_inc(w1_zeroed, 1)
            for u in range(SUBS):
                evacuate(copy, dve.wait_ge, 1, 0, 0, u)
            dve.wait_ge(w_loaded, 64)
            step(0, 0, mlp=False)
            step(1, 1, fresh=True)
            step(2, 0, fresh=True)
            step(3, 1)
            with dve.Fori(2, TILES // 2 - 1) as i:
                step(2 * i, 0)
                step(2 * i + 1, 1)
            step(TILES - 2, 0)
            step(TILES - 1, 1, turn=False)
            step(TILES, 0, turn=False, dots=False)


N_FIELDS = 32


def kernel(**inputs):
    import numpy as np
    import concourse.bacc as bacc
    from concourse.bass_utils import run_bass_kernel_spmd

    nc = bacc.Bacc("TRN2", target_bir_lowering=False, num_devices=1)
    arrays = {}

    def dram(name, a):
        a = np.ascontiguousarray(a)
        arrays[f"in_{name}"] = a
        return nc.dram_tensor(f"in_{name}", a.shape, mybir.dt.from_np(a.dtype), kind="ExternalInput").ap()

    dense_t = dram("dense_t", np.asarray(inputs["dense_ctx"]).T)
    ids = dram("ids", inputs["ids"])
    tables = [dram(f"tbl_{f}", inputs[f"tbl_{f}"]) for f in range(N_FIELDS)]
    w1, w2 = dram("W_top1", inputs["W_top1"]), dram("W_top2", inputs["W_top2"])
    b1_t, b2_t, w3_t = (dram(n, np.asarray(inputs[n]).reshape(-1, P).T) for n in ("b_top1", "b_top2", "W_top3"))
    out = nc.dram_tensor("scores", (ids.shape[0], 1), F32, kind="ExternalOutput").ap()
    dlrm_tower(nc, dense_t, ids, tables, w1, b1_t, w2, b2_t, w3_t, out)
    result = run_bass_kernel_spmd(nc, [arrays], core_ids=[0])
    return result.results[0]["scores"]
```

```python
from contextlib import ExitStack

import concourse.bass as bass
from concourse import mybir

F32 = mybir.dt.float32
F32R = mybir.dt.float32r
I32 = mybir.dt.int32
U32 = mybir.dt.uint32
ALU = mybir.AluOpType
ACT = mybir.ActivationFunctionType

P = 128


def dlrm_tower(nc, dense_t, ids, last_ids, tables, w1, b1_t, w2, b2_t, w3_t, out):
    NB, NF = ids.shape
    D = tables[0].shape[1]
    ND = dense_t.shape[0]
    H1, H2 = w2.shape
    TILES = NB // P
    HALVES = D // P
    FPS = 4
    SUBS = NF // FPS
    QUADS = P // NF
    FILLS = 4
    GPF = P // QUADS // FILLS // 2
    KC = NF // QUADS
    M1C, M2C = H1 // P, H2 // P
    LAST = NF - 1
    V = tables[LAST].shape[0]
    VC = 8
    VP = V // VC
    PICKED = LAST % FPS
    assert HALVES == 2 and NF == 32 and TILES % 2 == 0 and TILES >= 6
    assert GPF * P == 512 and 2 * FILLS == SUBS == 2 * M1C and VP * VC == V and VP <= P

    with ExitStack() as ctx:
        def sb(name, shape, dt=F32):
            return ctx.enter_context(nc.sbuf_tensor(name, shape, dt))

        def pb(name, shape):
            return ctx.enter_context(nc.psum_tensor(name, shape, F32))

        def sem(name):
            return ctx.enter_context(nc.semaphore(name))

        index = [sb(f"index{p}", [P, NF], U32) for p in range(2)]
        rows = [sb(f"rows{p}", [P, NF, D]) for p in range(2)]
        cols = [sb(f"cols{p}", [P, HALVES, P, NF]) for p in range(2)]
        pairs = [sb(f"pairs{p}", [P, KC, P]) for p in range(2)]
        hidden1 = sb("hidden1", [P, M1C, P])
        hidden2 = sb("hidden2", [P, M2C, P])
        score = [sb(f"score{p}", [P, 1]) for p in range(2)]
        w1_sb = sb("w1_sb", [P, KC, H1])
        w2_sb = sb("w2_sb", [P, M1C, H2])
        w3_sb = sb("w3_sb", [P, M2C])
        b1_sb = sb("b1_sb", [P, M1C])
        b2_sb = sb("b2_sb", [P, M2C])
        identity = sb("identity", [P, P])
        row_number = sb("row_number", [VP, VC])
        last_id = [sb(f"last_id{p}", [VP, P], I32) for p in range(2)]
        one_hot = sb("one_hot", [VP, VC, P], F32R)
        table_hi = sb("table_hi", [VP, VC, D], F32R)
        table_lo = sb("table_lo", [VP, VC, D], F32R)
        table_raw = cols[1][0:VP, 1, :, :].rearrange("p b f -> p (b f)")[:, 0:VC * D]\
            .rearrange("p (c d) -> p c d", c=VC)

        ps_turn = [[pb(f"ps_turn{c}{k}", [P, FPS, P]) for k in range(2)] for c in range(HALVES)]
        ps_gram = [pb(f"ps_gram{h}", [P, GPF, QUADS, NF - 1]) for h in range(2)]
        ps_l1 = pb("ps_l1", [P, M1C, P])
        ps_l23 = pb("ps_l23", [P, 512])

        index_loaded = [sem(f"index_loaded{p}") for p in range(2)]
        gathered = [[sem(f"gathered{p}_{u}") for u in range(SUBS)] for p in range(2)]
        transposed = [sem(f"transposed{c}") for c in range(HALVES)]
        cols_ready = [sem(f"cols_ready{c}") for c in range(HALVES)]
        gram_done = [sem(f"gram_done{h}") for h in range(2)]
        pairs_ready = [sem(f"pairs_ready{h}") for h in range(2)]
        dense_loaded = [sem(f"dense_loaded{p}") for p in range(2)]
        l1_done, l2_done, l3_done = sem("l1_done"), sem("l2_done"), sem("l3_done")
        hidden1_ready, hidden2_ready, score_ready = sem("hidden1_ready"), sem("hidden2_ready"), sem("score_ready")
        stored = [sem(f"stored{p}") for p in range(2)]
        gather_started = sem("gather_started")
        identity_zeroed, identity_ready = sem("identity_zeroed"), sem("identity_ready")
        w1_zeroed, pairs_zeroed = sem("w1_zeroed"), sem("pairs_zeroed")
        w1_loaded, w_loaded = sem("w1_loaded"), sem("w_loaded")
        table_loaded, hi_ready, table_ready = sem("table_loaded"), sem("hi_ready"), sem("table_ready")
        numbers_ready = sem("numbers_ready")
        last_id_loaded = [sem(f"last_id_loaded{p}") for p in range(2)]
        one_hot_ready, picked, picked_ready = sem("one_hot_ready"), sem("picked"), sem("picked_ready")

        block = ctx.enter_context(nc.Block())

        w1_loads = []
        for i in range(NF):
            first = i * (2 * NF - 1 - i) // 2
            for q in range(QUADS):
                c0 = max(0, i + 1 - KC * q)
                if c0 < KC:
                    w1_loads.append((NF * q + i, c0, first + KC * q + c0 - i - 1, KC - c0))
        N_PAIRS = NF * (NF - 1) // 2
        W1_TOTAL = 16 * (len(w1_loads) + 1)

        out_v = out.rearrange("(t p) o -> t p o", p=P)
        ids_v = ids.rearrange("(t p) f -> t p f", p=P)
        last_ids_v = last_ids.rearrange("(t o b) -> t o b", o=1, b=P)
        dense_v = dense_t.rearrange("d (t b) -> t d b", b=P)

        @block.sync
        def _(sp):
            def load_index(n, p):
                sp.dma_start(index[p][:, :], ids_v[n].bitcast(U32)).then_inc(index_loaded[p], 16)

            def load_last_id(n, p):
                sp.dma_start(last_id[p][:, :], last_ids_v[n].broadcast_to([VP, P])).then_inc(last_id_loaded[p], 16)

            def load_dense(n, p):
                sp.dma_start(pairs[p][0:ND, 0, :], dense_v[n]).then_inc(dense_loaded[p], 16)

            def store(n, p):
                sp.wait_ge(score_ready, n + 1)
                sp.dma_start(out_v[n], score[p][:, :]).then_inc(stored[p], 16)

            load_index(0, 0)
            load_index(1, 1)
            sp.dma_start(table_raw, tables[LAST].rearrange("(p c) d -> p c d", c=VC)).then_inc(table_loaded, 16)
            load_last_id(0, 0)
            load_last_id(1, 1)
            sp.dma_start(b1_sb[:, :], b1_t).then_inc(w_loaded, 16)
            sp.dma_start(b2_sb[:, :], b2_t).then_inc(w_loaded, 16)
            sp.dma_start(w3_sb[:, :], w3_t).then_inc(w_loaded, 16)
            sp.dma_start(w2_sb[:, :, :], w2.rearrange("(m p) n -> p m n", p=P)).then_inc(w_loaded, 16)
            sp.wait_ge(pairs_zeroed, 1)
            load_dense(0, 0)
            load_dense(1, 1)
            sp.wait_ge(w1_zeroed, 1)
            for part, c0, row, n in w1_loads:
                sp.dma_start(w1_sb[part:part + 1, c0:c0 + n, :],
                             w1[row:row + n, :].rearrange("(a c) n -> a c n", a=1)).then_inc(w1_loaded, 16)
            sp.dma_start(w1_sb[0:ND, 0, :], w1[N_PAIRS:N_PAIRS + ND, :]).then_inc(w1_loaded, 16)

            def refill_indices(n, p):
                sp.wait_ge(transposed[1], SUBS * (n - 1))
                load_index(n, p)
                sp.wait_ge(one_hot_ready, n - 1)
                load_last_id(n, p)

            def refill_dense(n, p):
                sp.wait_ge(l1_done, n - 1)
                load_dense(n, p)

            def step(n, p):
                refill_indices(n + 2, p)
                refill_dense(n, p)
                store(n - 2, p)

            refill_indices(2, 0)
            refill_indices(3, 1)
            with sp.Fori(1, TILES // 2 - 1) as i:
                step(2 * i, 0)
                step(2 * i + 1, 1)
            for n in (TILES - 2, TILES - 1):
                refill_dense(n, n % 2)
                store(n - 2, n % 2)
            store(TILES - 2, 0)
            store(TILES - 1, 1)
            for p in range(2):
                sp.wait_ge(stored[p], 16 * (TILES // 2))

        @block.gpsimd
        def _(pool):
            def gather_tile(n, p):
                pool.wait_ge(index_loaded[p], 8 * (n - p) + 16)
                pool.sem_inc(gather_started, 1)
                for field in range(LAST):
                    pool.indirect_dma_start(
                        out=rows[p][:, field, :], out_offset=None, in_=tables[field],
                        in_offset=bass.IndirectOffsetOnAxis(ap=index[p][:, field:field + 1], axis=0),
                    ).then_inc(gathered[p][field // FPS], 16)

            pool.memset(identity[:, :], 0.0).then_inc(identity_zeroed, 1)
            pool.iota(row_number[:, :], [[1, VC]], base=0, channel_multiplier=VC,
                      allow_small_or_imprecise_dtypes=True).then_inc(numbers_ready, 1)
            pool.wait_ge(identity_zeroed, 1)
            pool.affine_select(out=identity[:, :], in_=identity[:, :], compare_op=ALU.not_equal, fill=1.0,
                               base=0, pattern=[[-1, P]], channel_multiplier=1).then_inc(identity_ready, 1)
            gather_tile(0, 0)
            gather_tile(1, 1)
            with pool.Fori(1, TILES // 2) as i:
                gather_tile(2 * i, 0)
                gather_tile(2 * i + 1, 1)

        @block.tensor
        def _(pe):
            def transposes(n, p, u, fresh=False):
                gathers = FPS if u < SUBS - 1 else PICKED
                pe.wait_ge(gathered[p][u], gathers * (8 * (n - p) + 16))
                if u == SUBS - 1:
                    pe.wait_ge(picked_ready, n + 1)
                for c in range(HALVES):
                    if not fresh or u >= 2:
                        pe.wait_ge(cols_ready[c], SUBS * n + u - 1)
                    for f in range(FPS):
                        last = pe.transpose(ps_turn[c][u % 2][:, f, :],
                                            rows[p][:, FPS * u + f, c * P:(c + 1) * P], identity[:, :])
                    last.then_inc(transposed[c], 1)

            def pick(n, first=False):
                pe.wait_ge(one_hot_ready, n + 1)
                if first:
                    pe.wait_ge(table_ready, 1)
                for c in range(VC):
                    pe.matmul(ps_l23[:, 0:D], one_hot[:, c, :], table_hi[:, c, :], start=(c == 0), stop=False)
                    last = pe.matmul(ps_l23[:, 0:D], one_hot[:, c, :], table_lo[:, c, :],
                                     start=False, stop=(c == VC - 1))
                last.then_inc(picked, 1)

            def gram(n, p, u, h, fresh=False):
                if u == 0 and h == 0:
                    for c in range(HALVES):
                        pe.wait_ge(cols_ready[c], SUBS * (n + 1))
                if not fresh or u > 0:
                    pe.wait_ge(pairs_ready[h], FILLS * n + u)
                for g in range(GPF):
                    b = QUADS * (GPF * (2 * u + h) + g)
                    for c in range(HALVES):
                        last = pe.matmul(ps_gram[h][:, g, :, :], cols[p][:, c, b:b + QUADS, :],
                                         cols[p][:, c, b:b + QUADS, 1:NF], start=(c == 0), stop=(c == HALVES - 1))
                last.then_inc(gram_done[h], 1)

            def layer1(n, p, m, first=False):
                if m == 0:
                    for h in range(2):
                        pe.wait_ge(pairs_ready[h], FILLS * (n + 1))
                    pe.wait_ge(dense_loaded[p], 8 * (n - p) + 16)
                    if first:
                        pe.wait_ge(w1_loaded, W1_TOTAL)
                    else:
                        pe.wait_ge(hidden1_ready, n)
                for c in range(KC):
                    last = pe.matmul(ps_l1[:, m, :], w1_sb[:, c, m * P:(m + 1) * P], pairs[p][:, c, :],
                                     start=(c == 0), stop=(c == KC - 1))
                if m == M1C - 1:
                    last.then_inc(l1_done, 1)

            def layer2(n, first=False, final=False):
                pe.wait_ge(hidden1_ready, n + 1)
                if first:
                    pe.wait_ge(w_loaded, 64)
                if final:
                    pe.wait_ge(score_ready, n)
                else:
                    pe.wait_ge(picked_ready, n + 2)
                for m in range(M2C):
                    for c in range(M1C):
                        last = pe.matmul(ps_l23[:, m * P:(m + 1) * P], w2_sb[:, c, m * P:(m + 1) * P],
                                         hidden1[:, c, :], start=(c == 0), stop=(c == M1C - 1))
                last.then_inc(l2_done, 1)

            def layer3(n):
                pe.wait_ge(hidden2_ready, n + 1)
                for m in range(M2C):
                    last = pe.matmul(ps_l23[:, H2:H2 + 1], hidden2[:, m, :], w3_sb[:, m:m + 1],
                                     start=(m == 0), stop=(m == M2C - 1))
                last.then_inc(l3_done, 1)

            def step(n, p, fresh=False, mlp=True, first_mlp=False, final=False):
                for u in range(SUBS):
                    if not final:
                        transposes(n + 1, 1 - p, u)
                    if u < FILLS:
                        for h in range(2):
                            gram(n, p, u, h, fresh)
                    if mlp and u == 1:
                        layer2(n - 1, first_mlp, final)
                    if mlp and u == 2:
                        layer3(n - 1)
                    if not final and u == FILLS:
                        if mlp:
                            pe.wait_ge(score_ready, n)
                        pick(n + 1)
                    if u >= FILLS:
                        layer1(n, p, u - FILLS, fresh)

            pe.wait_ge(identity_ready, 1)
            pick(0, first=True)
            for u in range(SUBS):
                transposes(0, 0, u, fresh=True)
            pe.wait_ge(picked_ready, 1)
            step(0, 0, fresh=True, mlp=False)
            step(1, 1, first_mlp=True)
            with pe.Fori(1, TILES // 2 - 1) as i:
                step(2 * i, 0)
                step(2 * i + 1, 1)
            step(TILES - 2, 0)
            step(TILES - 1, 1, final=True)
            layer2(TILES - 1, final=True)
            layer3(TILES - 1)

        def evacuate(copy, wait, c, n, p, u):
            wait(transposed[c], SUBS * n + u + 1)
            copy(cols[p][:, c, :, FPS * u:FPS * (u + 1)].rearrange("p b f -> p f b"),
                 ps_turn[c][u % 2][:, :, :]).then_inc(cols_ready[c], 1)

        def regroup(copy, wait, n, p, u, h):
            wait(gram_done[h], FILLS * n + u + 1)
            for q in range(QUADS):
                c0 = 1 if q == 0 else 0
                for j in range(QUADS):
                    b = QUADS * GPF * (2 * u + h) + j
                    last = copy(pairs[p][NF * q:NF * (q + 1), c0:KC, b:b + QUADS * (GPF - 1) + 1:QUADS]
                                .rearrange("p c g -> p g c"),
                                ps_gram[h][NF * j:NF * (j + 1), :, j, KC * q + c0 - 1:KC * (q + 1) - 1])
            last.then_inc(pairs_ready[h], 1)

        @block.scalar
        def _(act):
            def copy(dst, src):
                return act.copy(dst, src)

            def relu1(n, first=False):
                act.wait_ge(l1_done, n + 1)
                if first:
                    act.wait_ge(w_loaded, 64)
                for m in range(M1C):
                    last = act.activation(hidden1[:, m, :], ps_l1[:, m, :], ACT.Relu, bias=b1_sb[:, m:m + 1])
                last.then_inc(hidden1_ready, 1)

            def step(n, p, mlp=True, first_mlp=False, final=False):
                for u in range(SUBS):
                    if mlp and u == 0:
                        relu1(n - 1, first_mlp)
                    if not final:
                        evacuate(copy, act.wait_ge, 0, n + 1, 1 - p, u)
                    if u < FILLS:
                        regroup(copy, act.wait_ge, n, p, u, 1)

            act.wait_ge(pairs_zeroed, 1)
            for u in range(SUBS):
                evacuate(copy, act.wait_ge, 0, 0, 0, u)
            act.wait_ge(table_ready, 1)
            step(0, 0, mlp=False)
            step(1, 1, first_mlp=True)
            with act.Fori(1, TILES // 2 - 1) as i:
                step(2 * i, 0)
                step(2 * i + 1, 1)
            step(TILES - 2, 0)
            step(TILES - 1, 1, final=True)
            relu1(TILES - 1)

        @block.vector
        def _(dve):
            def copy(dst, src):
                return dve.tensor_copy(dst, src)

            def make_one_hot(n, p):
                dve.wait_ge(last_id_loaded[p], 8 * (n - p) + 16)
                dve.tensor_tensor(one_hot[:, :, :], last_id[p][:, :].unsqueeze(1).broadcast_to([VP, VC, P]),
                                  row_number[:, :].unsqueeze(2).broadcast_to([VP, VC, P]),
                                  ALU.is_equal).then_inc(one_hot_ready, 1)

            def take_picked(n, p):
                dve.wait_ge(picked, n + 1)
                dve.tensor_copy(rows[p][:, LAST, :], ps_l23[:, 0:D]).then_inc(picked_ready, 1)

            def relu2(n):
                dve.wait_ge(l2_done, n + 1)
                for m in range(M2C):
                    last = dve.tensor_scalar(hidden2[:, m, :], ps_l23[:, m * P:(m + 1) * P], b2_sb[:, m:m + 1],
                                             0.0, ALU.add, ALU.max)
                last.then_inc(hidden2_ready, 1)

            def take_score(n, p, fresh=False):
                dve.wait_ge(l3_done, n + 1)
                if not fresh:
                    dve.wait_ge(stored[p], 8 * (n - p))
                dve.tensor_copy(score[p][:, :], ps_l23[:, H2:H2 + 1]).then_inc(score_ready, 1)

            def step(n, p, mlp=True, fresh=False, final=False, one_hot_next=True):
                for u in range(SUBS):
                    if not final:
                        evacuate(copy, dve.wait_ge, 1, n + 1, 1 - p, u)
                    if mlp and u == 2:
                        relu2(n - 1)
                    if mlp and u == 3:
                        take_score(n - 1, 1 - p, fresh)
                    if not final and u == FILLS + 1:
                        take_picked(n + 1, 1 - p)
                        if one_hot_next:
                            make_one_hot(n + 2, p)
                    if u < FILLS:
                        regroup(copy, dve.wait_ge, n, p, u, 0)

            for p in range(2):
                last = dve.memset(pairs[p][0:NF, 0, :], 0.0)
            last.then_inc(pairs_zeroed, 1)
            dve.memset(w1_sb[:, :, :], 0.0).then_inc(w1_zeroed, 1)
            dve.wait_ge(numbers_ready, 1)
            make_one_hot(0, 0)
            dve.wait_ge(table_loaded, 16)
            dve.tensor_copy(table_hi[:, :, :], table_raw).then_inc(hi_ready, 1)
            dve.wait_ge(hi_ready, 1)
            dve.tensor_tensor(table_lo[:, :, :], table_raw, table_hi[:, :, :], ALU.subtract).then_inc(table_ready, 1)
            take_picked(0, 0)
            make_one_hot(1, 1)
            for u in range(SUBS):
                evacuate(copy, dve.wait_ge, 1, 0, 0, u)
            dve.wait_ge(w_loaded, 64)
            step(0, 0, mlp=False)
            step(1, 1, fresh=True)
            step(2, 0, fresh=True)
            step(3, 1)
            with dve.Fori(2, TILES // 2 - 1) as i:
                step(2 * i, 0)
                step(2 * i + 1, 1)
            step(TILES - 2, 0, one_hot_next=False)
            step(TILES - 1, 1, final=True)
            relu2(TILES - 1)
            take_score(TILES - 1, 1)


N_FIELDS = 32


def kernel(**inputs):
    import numpy as np
    import concourse.bacc as bacc
    from concourse.bass_utils import run_bass_kernel_spmd

    nc = bacc.Bacc("TRN2", target_bir_lowering=False, num_devices=1)
    arrays = {}

    def dram(name, a):
        a = np.ascontiguousarray(a)
        arrays[f"in_{name}"] = a
        return nc.dram_tensor(f"in_{name}", a.shape, mybir.dt.from_np(a.dtype), kind="ExternalInput").ap()

    dense_t = dram("dense_t", np.asarray(inputs["dense_ctx"]).T)
    ids = dram("ids", inputs["ids"])
    last_ids = dram("last_ids", np.asarray(inputs["ids"])[:, N_FIELDS - 1])
    tables = [dram(f"tbl_{f}", inputs[f"tbl_{f}"]) for f in range(N_FIELDS)]
    w1, w2 = dram("W_top1", inputs["W_top1"]), dram("W_top2", inputs["W_top2"])
    b1_t, b2_t, w3_t = (dram(n, np.asarray(inputs[n]).reshape(-1, P).T) for n in ("b_top1", "b_top2", "W_top3"))
    out = nc.dram_tensor("scores", (ids.shape[0], 1), F32, kind="ExternalOutput").ap()
    dlrm_tower(nc, dense_t, ids, last_ids, tables, w1, b1_t, w2, b2_t, w3_t, out)
    result = run_bass_kernel_spmd(nc, [arrays], core_ids=[0])
    return result.results[0]["scores"]
```

```python
from contextlib import ExitStack

import concourse.bass as bass
from concourse import mybir

F32 = mybir.dt.float32
F32R = mybir.dt.float32r
I32 = mybir.dt.int32
U32 = mybir.dt.uint32
ALU = mybir.AluOpType
ACT = mybir.ActivationFunctionType

P = 128


def dlrm_tower(nc, dense_t, ids, last_ids, tables, w1, b1_t, w2, b2_t, w3_t, out):
    NB, NF = ids.shape
    D = tables[0].shape[1]
    ND = dense_t.shape[0]
    H1, H2 = w2.shape
    TILES = NB // P
    HALVES = D // P
    FPS = 4
    SUBS = NF // FPS
    QUADS = P // NF
    FILLS = 4
    GPF = P // QUADS // FILLS // 2
    KS = 8
    KC = (NF - KS) // QUADS
    STAGED = KS - 1
    M1C, M2C = H1 // P, H2 // P
    PICKS = last_ids.shape[0]
    PICKED_2 = 2
    V = tables[-1].shape[0]
    VC = 8
    VP = V // VC
    SQ = 32
    SQUARES = (P // SQ) ** 2
    SQF = (8, 8)
    SQ0 = (0, SQF[0])
    FIRST = sum(SQF) // FPS
    TURNS = SUBS - FIRST
    assert FIRST == SUBS // 2 and ND == 2 * KS == P // QUADS // 2
    assert HALVES == 2 and NF == 32 and TILES % 2 == 0 and TILES >= 6
    assert GPF * P == 512 and 2 * FILLS == SUBS == 2 * M1C and VP * VC == V and VP <= P
    assert PICKS == 3 and PICKED_2 * D == 512 and all(t.shape[0] == V for t in tables[NF - PICKS:])

    with ExitStack() as ctx:
        def sb(name, shape, dt=F32):
            return ctx.enter_context(nc.sbuf_tensor(name, shape, dt))

        def pb(name, shape):
            return ctx.enter_context(nc.psum_tensor(name, shape, F32))

        def sem(name):
            return ctx.enter_context(nc.semaphore(name))

        index = [sb(f"index{p}", [P, NF], U32) for p in range(2)]
        rows = sb("rows", [P, NF, D])
        cols = [sb(f"cols{p}", [P, HALVES, P, NF]) for p in range(2)]
        pairs = sb("pairs", [P, STAGED + KC, P])
        hidden1 = sb("hidden1", [P, M1C, P])
        hidden2 = sb("hidden2", [P, M2C, P])
        score = [sb(f"score{p}", [P, 1]) for p in range(2)]
        w1_sb = sb("w1_sb", [P, KC, H1])
        w2_sb = sb("w2_sb", [P, M1C, H2])
        w3_sb = sb("w3_sb", [P, M2C])
        b1_sb = sb("b1_sb", [P, M1C])
        b2_sb = sb("b2_sb", [P, M2C])
        identity = sb("identity", [P, P])
        row_number = sb("row_number", [VP, VC])
        last_id = [sb(f"last_id{p}", [VP, PICKS, P], I32) for p in range(2)]
        one_hot = sb("one_hot", [VP, PICKS, VC, P], F32R)
        table_hi = sb("table_hi", [VP, PICKS, VC, D], F32R)
        table_lo = sb("table_lo", [VP, PICKS, VC, D], F32R)
        table_raw = cols[1][0:VP, :, :, :].rearrange("p c b f -> p (c b f)")[:, 0:PICKS * VC * D]\
            .rearrange("p (t c d) -> p t c d", t=PICKS, c=VC)

        ps_turn = [pb(f"ps_turn{k}", [P, HALVES, FPS, P]) for k in range(2)]
        ps_gram = [pb(f"ps_gram{h}", [P, GPF, QUADS, NF - 1]) for h in range(2)]
        ps_l1 = pb("ps_l1", [P, M1C, P])
        ps_l23 = pb("ps_l23", [P, 512])

        ps_last_gram = [ps_turn[1][:, h, :, 0:QUADS * (NF - 1)].rearrange("p g (j k) -> p g j k", j=QUADS)
                        for h in range(2)]
        ps_last_l1 = [ps_turn[0][:, 0, 0, :], ps_turn[0][:, 1, 0, :], ps_l1[:, 0, :], ps_turn[1][:, 0, 0, :]]
        ps_last_l2 = [ps_l23[:, 0:P], ps_gram[0][:, :, :, :].rearrange("p g j k -> p (g j k)")[:, 0:P]]

        index_loaded = [sem(f"index_loaded{p}") for p in range(2)]
        gathered = [sem(f"gathered{u}") for u in range(SUBS)]
        transposed = sem("transposed")
        cols_ready = sem("cols_ready")
        squares_ready = [sem(f"squares_ready{i}") for i in range(2)]
        first_transposed, first_evacuated = sem("first_transposed"), sem("first_evacuated")
        gram_done = [sem(f"gram_done{h}") for h in range(2)]
        pairs_ready = [sem(f"pairs_ready{h}") for h in range(2)]
        dense_loaded, moved = sem("dense_loaded"), sem("moved")
        l1_done, l2_done, l3_done = sem("l1_done"), sem("l2_done"), sem("l3_done")
        l1_last_done = sem("l1_last_done")
        last_hidden1_ready = sem("last_hidden1_ready")
        l2_last_done, last_hidden2_ready = sem("l2_last_done"), sem("last_hidden2_ready")
        hidden1_ready, hidden2_ready, score_ready = sem("hidden1_ready"), sem("hidden2_ready"), sem("score_ready")
        stored = [sem(f"stored{p}") for p in range(2)]
        gather_started = sem("gather_started")
        identity_zeroed, identity_ready = sem("identity_zeroed"), sem("identity_ready")
        w1_zeroed, pairs_zeroed = sem("w1_zeroed"), sem("pairs_zeroed")
        w1_loaded, w_loaded = sem("w1_loaded"), sem("w_loaded")
        table_loaded, hi_ready, table_ready = sem("table_loaded"), sem("hi_ready"), sem("table_ready")
        numbers_ready = sem("numbers_ready")
        last_id_loaded = [sem(f"last_id_loaded{p}") for p in range(2)]
        one_hot_ready = sem("one_hot_ready")
        picked, picked_ready = sem("picked"), sem("picked_ready")
        last_picked, last_picked_ready = sem("last_picked"), sem("last_picked_ready")

        block = ctx.enter_context(nc.Block())

        w1_loads = []
        for i in range(NF):
            first = i * (2 * NF - 1 - i) // 2
            for part, k0, slot0, n in ([(NF // 2 + i, 1, 2, 4), (NF // 2 + KS + i, 5, 3, 3)] +
                                       [(NF * q + i, KS + KC * q, 0, KC) for q in range(QUADS)]):
                skip = max(0, i + 1 - k0)
                if skip < n:
                    w1_loads.append((part, slot0 + skip, first + k0 + skip - i - 1, n - skip))
        N_PAIRS = NF * (NF - 1) // 2
        W1_TOTAL = 16 * (len(w1_loads) + 1)

        out_v = out.rearrange("(t p) o -> t p o", p=P)
        ids_v = ids.rearrange("(t p) f -> t p f", p=P)
        last_ids_v = last_ids.rearrange("f (t b) -> t f b", b=P)
        dense_v = dense_t.rearrange("d (t b) -> t d b", b=P)

        @block.sync
        def _(sp):
            def load_index(n, p):
                sp.dma_start(index[p][:, :], ids_v[n].bitcast(U32)).then_inc(index_loaded[p], 16)

            def load_last_id(n, p):
                sp.dma_start(last_id[p][:, :], last_ids_v[n].unsqueeze(0).broadcast_to([VP, PICKS, P])
                             ).then_inc(last_id_loaded[p], 16)

            def load_dense(n):
                sp.dma_start(pairs[NF // 2:NF, STAGED, :], dense_v[n]).then_inc(dense_loaded, 16)

            def move_pairs(n):
                for h in range(2):
                    sp.wait_ge(pairs_ready[h], FILLS * (n + 1))
                for part, k0, chunk0, n_k in ((NF // 2, 1, 2, 4), (NF // 2 + KS, 5, 3, 3)):
                    sp.dma_start(pairs[part:part + KS, STAGED + chunk0:STAGED + chunk0 + n_k, :],
                                 pairs[0:KS, k0 - 1:k0 - 1 + n_k, :]).then_inc(moved, 16)

            def store(n, p):
                sp.wait_ge(score_ready, n + 1)
                sp.dma_start(out_v[n], score[p][:, :]).then_inc(stored[p], 16)

            load_index(0, 0)
            load_index(1, 1)
            for t in range(PICKS):
                sp.dma_start(table_raw[:, t, :, :], tables[NF - PICKS + t].rearrange("(p c) d -> p c d", c=VC)
                             ).then_inc(table_loaded, 16)
            load_last_id(0, 0)
            load_last_id(1, 1)
            sp.dma_start(b1_sb[:, :], b1_t).then_inc(w_loaded, 16)
            sp.dma_start(b2_sb[:, :], b2_t).then_inc(w_loaded, 16)
            sp.dma_start(w3_sb[:, :], w3_t).then_inc(w_loaded, 16)
            sp.dma_start(w2_sb[:, :, :], w2.rearrange("(m p) n -> p m n", p=P)).then_inc(w_loaded, 16)
            sp.wait_ge(pairs_zeroed, 1)
            load_dense(0)
            sp.wait_ge(w1_zeroed, 1)
            for part, c0, row, n in w1_loads:
                sp.dma_start(w1_sb[part:part + 1, c0:c0 + n, :],
                             w1[row:row + n, :].rearrange("(a c) n -> a c n", a=1)).then_inc(w1_loaded, 16)
            sp.dma_start(w1_sb[NF // 2:NF, 0, :], w1[N_PAIRS:N_PAIRS + ND, :]).then_inc(w1_loaded, 16)

            def refill_indices(n, p, first=False):
                sp.wait_ge(transposed, TURNS * (n - 1))
                if first:
                    sp.wait_ge(first_evacuated, FIRST)
                for i in range(2):
                    if not first:
                        sp.wait_ge(squares_ready[i], n - 2)
                load_index(n, p)
                sp.wait_ge(one_hot_ready, n - 1)
                load_last_id(n, p)

            def step(n, p, refill=True, store_last=True):
                if store_last:
                    store(n - 2, p)
                move_pairs(n)
                sp.wait_ge(l1_done, n + 1)
                load_dense(n + 1)
                if refill:
                    refill_indices(n + 3, 1 - p)

            refill_indices(2, 0, first=True)
            step(0, 0, store_last=False)
            step(1, 1, store_last=False)
            with sp.Fori(1, TILES // 2 - 2) as i:
                step(2 * i, 0)
                step(2 * i + 1, 1)
            step(TILES - 4, 0)
            step(TILES - 3, 1, refill=False)
            step(TILES - 2, 0, refill=False)
            store(TILES - 3, 1)
            move_pairs(TILES - 1)
            store(TILES - 2, 0)
            store(TILES - 1, 1)
            for p in range(2):
                sp.wait_ge(stored[p], 16 * (TILES // 2))

        @block.gpsimd
        def _(pool):
            def gather(p, u):
                for field in range(FPS * u, min(FPS * (u + 1), NF - PICKS)):
                    pool.indirect_dma_start(
                        out=rows[:, field, :], out_offset=None, in_=tables[field],
                        in_offset=bass.IndirectOffsetOnAxis(ap=index[p][:, field:field + 1], axis=0),
                    ).then_inc(gathered[u], 16)

            def gather_tile(n, p, fresh=False, second=False):
                if second:
                    pool.wait_ge(first_evacuated, SQ0[1] // FPS)
                elif not fresh:
                    pool.wait_ge(squares_ready[0], n - 1)
                pool.wait_ge(index_loaded[p], 8 * (n - p) + 16)
                pool.sem_inc(gather_started, 1)
                for u in range(SQ0[1] // FPS):
                    gather(p, u)
                if second:
                    pool.wait_ge(first_evacuated, FIRST)
                elif not fresh:
                    pool.wait_ge(squares_ready[1], n - 1)
                    pool.sem_inc(gather_started, 1)
                for u in range(SQ0[1] // FPS, SUBS // 2):
                    gather(p, u)
                if not fresh:
                    pool.wait_ge(transposed, TURNS * n)
                    pool.sem_inc(gather_started, 1)
                for u in range(SUBS // 2, SUBS):
                    gather(p, u)

            pool.memset(identity[:, :], 0.0).then_inc(identity_zeroed, 1)
            pool.iota(row_number[:, :], [[1, VC]], base=0, channel_multiplier=VC,
                      allow_small_or_imprecise_dtypes=True).then_inc(numbers_ready, 1)
            pool.wait_ge(identity_zeroed, 1)
            pool.affine_select(out=identity[:, :], in_=identity[:, :], compare_op=ALU.not_equal, fill=1.0,
                               base=0, pattern=[[-1, P]], channel_multiplier=1).then_inc(identity_ready, 1)
            gather_tile(0, 0, fresh=True)
            gather_tile(1, 1, second=True)
            with pool.Fori(1, TILES // 2) as i:
                gather_tile(2 * i, 0)
                gather_tile(2 * i + 1, 1)

        @block.tensor
        def _(pe):
            def transpose_group(u):
                for c in range(HALVES):
                    for f in range(FPS):
                        last = pe.transpose(ps_turn[u % 2][:, c, f, :],
                                            rows[:, FPS * u + f, c * P:(c + 1) * P], identity[:, :])
                return last

            def first_transposes(u):
                pe.wait_ge(gathered[u], 16 * FPS)
                if u >= 2:
                    pe.wait_ge(first_evacuated, u - 1)
                transpose_group(u).then_inc(first_transposed, 1)

            def transposes(n, u, fresh=False):
                turn = u - FIRST
                gathers = min(FPS, NF - PICKS - FPS * u)
                pe.wait_ge(gathered[u], 16 * gathers * (n + 1))
                if u == SUBS - 1:
                    pe.wait_ge(picked_ready, n + 1)
                    pe.wait_ge(last_picked_ready, n + 1)
                if fresh and turn < 2:
                    pe.wait_ge(first_evacuated, FIRST - 1 + turn)
                else:
                    pe.wait_ge(cols_ready, TURNS * n + turn - 1)
                transpose_group(u).then_inc(transposed, 1)

            def pick(n, t, first=False):
                pe.wait_ge(one_hot_ready, n + 1)
                if first:
                    pe.wait_ge(table_ready, 1)
                bank = ps_l23[:, t * D:(t + 1) * D] if t < PICKED_2 else ps_l1[:, 0:D // P, :]
                for c in range(VC):
                    pe.matmul(bank, one_hot[:, t, c, :], table_hi[:, t, c, :], start=(c == 0), stop=False)
                    last = pe.matmul(bank, one_hot[:, t, c, :], table_lo[:, t, c, :],
                                     start=False, stop=(c == VC - 1))
                if t == PICKED_2 - 1:
                    last.then_inc(picked, 1)
                if t == PICKS - 1:
                    last.then_inc(last_picked, 1)

            def gram(n, p, u, h, fresh=False, last=False):
                if u == 0 and h == 0:
                    pe.wait_ge(cols_ready, TURNS * (n + 1))
                    if fresh:
                        pe.wait_ge(first_evacuated, FIRST)
                    else:
                        for i in range(2):
                            pe.wait_ge(squares_ready[i], n)
                bank = ps_last_gram[h] if last and u % 2 else ps_gram[h]
                if last and u > 0:
                    pe.wait_ge(pairs_ready[h], FILLS * n + u - 1)
                elif not fresh or u > 0:
                    pe.wait_ge(pairs_ready[h], FILLS * n + u)
                for g in range(GPF):
                    b = QUADS * (GPF * (2 * u + h) + g)
                    for c in range(HALVES):
                        done = pe.matmul(bank[:, g, :, :], cols[p][:, c, b:b + QUADS, :],
                                         cols[p][:, c, b:b + QUADS, 1:NF], start=(c == 0), stop=(c == HALVES - 1))
                done.then_inc(gram_done[h], 1)

            def layer1(n, m, first=False):
                if m == 0:
                    for h in range(2):
                        pe.wait_ge(pairs_ready[h], FILLS * (n + 1))
                    pe.wait_ge(dense_loaded, 16 * (n + 1))
                    pe.wait_ge(last_picked_ready, n + 2)
                    if first:
                        pe.wait_ge(w1_loaded, W1_TOTAL)
                for c in range(KC):
                    if m == 0 and c == 2:
                        pe.wait_ge(moved, 32 * (n + 1))
                    last = pe.matmul(ps_l1[:, m, :], w1_sb[:, c, m * P:(m + 1) * P], pairs[:, STAGED + c, :],
                                     start=(c == 0), stop=(c == KC - 1))
                if m == M1C - 1:
                    last.then_inc(l1_done, 1)

            def layer2(n, first=False):
                pe.wait_ge(hidden1_ready, n + 1)
                if first:
                    pe.wait_ge(w_loaded, 64)
                pe.wait_ge(picked_ready, n + 2)
                for m in range(M2C):
                    for c in range(M1C):
                        last = pe.matmul(ps_l23[:, m * P:(m + 1) * P], w2_sb[:, c, m * P:(m + 1) * P],
                                         hidden1[:, c, :], start=(c == 0), stop=(c == M1C - 1))
                last.then_inc(l2_done, 1)

            def layer3(n):
                pe.wait_ge(hidden2_ready, n + 1)
                for m in range(M2C):
                    last = pe.matmul(ps_l23[:, H2:H2 + 1], hidden2[:, m, :], w3_sb[:, m:m + 1],
                                     start=(m == 0), stop=(m == M2C - 1))
                last.then_inc(l3_done, 1)

            def step(n, p, fresh=False, mlp=True, first_mlp=False):
                for u in range(FILLS):
                    for h in range(2):
                        gram(n, p, u, h, fresh)
                    if mlp and u == 0:
                        layer2(n - 1, first_mlp)
                    if u == 1:
                        if mlp:
                            layer3(n - 1)
                            pe.wait_ge(hidden1_ready, n)
                        else:
                            pe.wait_ge(last_picked_ready, n + 1)
                        pick(n + 1, PICKS - 1)
                transposes(n + 1, FIRST)
                if mlp:
                    pe.wait_ge(score_ready, n)
                for t in range(PICKED_2):
                    pick(n + 1, t)
                for m in range(M1C):
                    layer1(n, m, fresh)
                    if m < 3:
                        transposes(n + 1, FIRST + 1 + m)

            def last_layer1(n, m, chunks):
                for c in chunks:
                    last = pe.matmul(ps_last_l1[m], w1_sb[:, c, m * P:(m + 1) * P], pairs[:, STAGED + c, :],
                                     start=(c == 0), stop=(c == KC - 1))
                if chunks.stop == KC:
                    last.then_inc(l1_last_done, 1)

            def last_layer2(c):
                pe.wait_ge(last_hidden1_ready, c + 1)
                for m in range(M2C):
                    last = pe.matmul(ps_last_l2[m], w2_sb[:, c, m * P:(m + 1) * P], hidden1[:, c, :],
                                     start=(c == 0), stop=(c == M1C - 1))
                    if c == M1C - 1:
                        last.then_inc(l2_last_done, 1)

            def last_layer3():
                for m in range(M2C):
                    pe.wait_ge(last_hidden2_ready, m + 1)
                    last = pe.matmul(ps_l23[:, H2:H2 + 1], hidden2[:, m, :], w3_sb[:, m:m + 1],
                                     start=(m == 0), stop=(m == M2C - 1))
                last.then_inc(l3_done, 1)

            def last_step(n, p):
                for u in range(FILLS):
                    for h in range(2):
                        gram(n, p, u, h, last=True)
                layer2(n - 1)
                for h in range(2):
                    pe.wait_ge(pairs_ready[h], FILLS * (n + 1))
                pe.wait_ge(dense_loaded, 16 * (n + 1))
                for m in range(M1C):
                    last_layer1(n, m, range(2))
                layer3(n - 1)
                pe.wait_ge(moved, 32 * (n + 1))
                for m in range(M1C - 1):
                    last_layer1(n, m, range(2, KC))
                pe.wait_ge(score_ready, n)
                last_layer2(0)
                last_layer1(n, M1C - 1, range(2, KC))
                for c in range(1, M1C):
                    last_layer2(c)
                last_layer3()

            pe.wait_ge(identity_ready, 1)
            for u in range(FIRST):
                first_transposes(u)
            for t in range(PICKS):
                pick(0, t, first=True)
            for u in range(FIRST, SUBS):
                transposes(0, u, fresh=True)
            step(0, 0, fresh=True, mlp=False)
            step(1, 1, first_mlp=True)
            with pe.Fori(1, TILES // 2 - 1) as i:
                step(2 * i, 0)
                step(2 * i + 1, 1)
            step(TILES - 2, 0)
            last_step(TILES - 1, 1)

        def regroup(copy, wait, n, u, h, last=False):
            wait(gram_done[h], FILLS * n + u + 1)
            bank = ps_last_gram[h] if last and u % 2 else ps_gram[h]
            for q in range(QUADS):
                rows_i, s0 = (NF // 2, 0) if q == 0 else (NF, STAGED)
                for j in range(QUADS):
                    b = QUADS * GPF * (2 * u + h) + j
                    done = copy(pairs[NF * q:NF * q + rows_i, s0:STAGED + KC, b:b + QUADS * (GPF - 1) + 1:QUADS]
                                .rearrange("p c g -> p g c"),
                                bank[NF * j:NF * j + rows_i, :, j, s0 + KC * q:STAGED + KC * (q + 1)])
            done.then_inc(pairs_ready[h], 1)

        @block.scalar
        def _(act):
            def copy(dst, src):
                return act.copy(dst, src)

            def relu1(n, first=False):
                act.wait_ge(l1_done, n + 1)
                if first:
                    act.wait_ge(w_loaded, 64)
                for m in range(M1C):
                    last = act.activation(hidden1[:, m, :], ps_l1[:, m, :], ACT.Relu, bias=b1_sb[:, m:m + 1])
                last.then_inc(hidden1_ready, 1)

            def evacuate(n, p, u):
                turn = u - FIRST
                act.wait_ge(transposed, TURNS * n + turn + 1)
                act.copy(cols[p][:, :, :, FPS * u:FPS * (u + 1)].rearrange("p c b f -> p c f b"),
                         ps_turn[turn % 2][:, :, :, :]).then_inc(cols_ready, 1)

            def step(n, p, mlp=True, first_mlp=False):
                if mlp:
                    relu1(n - 1, first_mlp)
                for u in range(FILLS):
                    if u > 0:
                        regroup(copy, act.wait_ge, n, u, 0)
                    regroup(copy, act.wait_ge, n, u, 1)
                    if u == 1:
                        take_last_picked(n + 1)
                for u in range(FIRST, SUBS):
                    evacuate(n + 1, 1 - p, u)

            def take_last_picked(n):
                act.wait_ge(last_picked, n + 1)
                act.copy(rows[:, NF - 1, :], ps_l1[:, 0:D // P, :].rearrange("p m b -> p (m b)")
                         ).then_inc(last_picked_ready, 1)

            for u in range(FIRST):
                act.wait_ge(first_transposed, u + 1)
                act.copy(cols[0][:, :, :, FPS * u:FPS * (u + 1)].rearrange("p c b f -> p c f b"),
                         ps_turn[u % 2][:, :, :, :]).then_inc(first_evacuated, 1)
            act.wait_ge(table_ready, 1)
            take_last_picked(0)
            for u in range(FIRST, SUBS):
                evacuate(0, 0, u)
            act.wait_ge(pairs_zeroed, 1)
            step(0, 0, mlp=False)
            step(1, 1, first_mlp=True)
            with act.Fori(1, TILES // 2 - 1) as i:
                step(2 * i, 0)
                step(2 * i + 1, 1)
            step(TILES - 2, 0)
            relu1(TILES - 2)
            for u in range(FILLS):
                regroup(copy, act.wait_ge, TILES - 1, u, 1, last=True)
            act.wait_ge(l2_done, TILES - 1)
            for m in range(M1C):
                act.wait_ge(l1_last_done, m + 1)
                act.activation(hidden1[:, m, :], ps_last_l1[m], ACT.Relu, bias=b1_sb[:, m:m + 1]
                               ).then_inc(last_hidden1_ready, 1)

        @block.vector
        def _(dve):
            def copy(dst, src):
                return dve.tensor_copy(dst, src)

            def make_one_hot(n, p):
                dve.wait_ge(last_id_loaded[p], 8 * (n - p) + 16)
                dve.tensor_tensor(one_hot[:, :, :, :], last_id[p][:, :, :].unsqueeze(2).broadcast_to([VP, PICKS, VC, P]),
                                  row_number[:, :].unsqueeze(1).unsqueeze(3).broadcast_to([VP, PICKS, VC, P]),
                                  ALU.is_equal).then_inc(one_hot_ready, 1)

            def take_picked(n):
                dve.wait_ge(picked, n + 1)
                dve.tensor_copy(rows[:, NF - PICKS:NF - PICKS + PICKED_2, :].rearrange("p f d -> p (f d)"),
                                ps_l23[:, 0:PICKED_2 * D]).then_inc(picked_ready, 1)

            def squares(n, p, i, first, last):
                if first == 0:
                    for u in range(SQ0[i] // FPS, (SQ0[i] + SQF[i]) // FPS):
                        dve.wait_ge(gathered[u], 16 * FPS * (n + 1))
                for s in range(first, last):
                    a, r = s // (P // SQ), s % (P // SQ)
                    src = rows[SQ * a:SQ * (a + 1), SQ0[i]:SQ0[i] + SQF[i], :]\
                        .rearrange("p f (h r d) -> p f h r d", h=HALVES, d=SQ)
                    done = dve.transpose(cols[p][SQ * r:SQ * (r + 1), :, SQ * a:SQ * (a + 1), SQ0[i]:SQ0[i] + SQF[i]]
                                         .rearrange("p h b f -> p f h b"), src[:, :, :, r, :])
                if last == SQUARES:
                    done.then_inc(squares_ready[i], 1)

            def relu2(n):
                dve.wait_ge(l2_done, n + 1)
                for m in range(M2C):
                    last = dve.tensor_scalar(hidden2[:, m, :], ps_l23[:, m * P:(m + 1) * P], b2_sb[:, m:m + 1],
                                             0.0, ALU.add, ALU.max)
                last.then_inc(hidden2_ready, 1)

            def take_score(n, p, fresh=False):
                dve.wait_ge(l3_done, n + 1)
                if not fresh:
                    dve.wait_ge(stored[p], 8 * (n - p))
                dve.tensor_copy(score[p][:, :], ps_l23[:, H2:H2 + 1]).then_inc(score_ready, 1)

            def step(n, p, mlp=True, fresh=False):
                regroup(copy, dve.wait_ge, n, 0, 0)
                make_one_hot(n + 1, 1 - p)
                if mlp:
                    relu2(n - 1)
                squares(n + 1, 1 - p, 0, 0, 5)
                if mlp:
                    take_score(n - 1, 1 - p, fresh)
                squares(n + 1, 1 - p, 0, 5, SQUARES)
                squares(n + 1, 1 - p, 1, 0, SQUARES // 2)
                take_picked(n + 1)
                squares(n + 1, 1 - p, 1, SQUARES // 2, SQUARES)

            dve.memset(pairs[0:NF, STAGED:STAGED + KC, :], 0.0).then_inc(pairs_zeroed, 1)
            dve.memset(w1_sb[:, :, :], 0.0).then_inc(w1_zeroed, 1)
            dve.wait_ge(numbers_ready, 1)
            make_one_hot(0, 0)
            dve.wait_ge(table_loaded, 16 * PICKS)
            dve.tensor_copy(table_hi[:, :, :, :], table_raw).then_inc(hi_ready, 1)
            dve.wait_ge(hi_ready, 1)
            dve.tensor_tensor(table_lo[:, :, :, :], table_raw, table_hi[:, :, :, :], ALU.subtract
                              ).then_inc(table_ready, 1)
            take_picked(0)
            dve.wait_ge(w_loaded, 64)
            step(0, 0, mlp=False)
            step(1, 1, fresh=True)
            step(2, 0, fresh=True)
            step(3, 1)
            with dve.Fori(2, TILES // 2 - 1) as i:
                step(2 * i, 0)
                step(2 * i + 1, 1)
            step(TILES - 2, 0)
            for u in range(FILLS):
                regroup(copy, dve.wait_ge, TILES - 1, u, 0, last=True)
            relu2(TILES - 2)
            take_score(TILES - 2, 0)
            for m in range(M2C):
                dve.wait_ge(l2_last_done, m + 1)
                dve.tensor_scalar(hidden2[:, m, :], ps_last_l2[m], b2_sb[:, m:m + 1], 0.0, ALU.add, ALU.max
                                  ).then_inc(last_hidden2_ready, 1)
            take_score(TILES - 1, 1)


N_FIELDS = 32
N_PICKED = 3


def kernel(**inputs):
    import numpy as np
    import concourse.bacc as bacc
    from concourse.bass_utils import run_bass_kernel_spmd

    nc = bacc.Bacc("TRN2", target_bir_lowering=False, num_devices=1)
    arrays = {}

    def dram(name, a):
        a = np.ascontiguousarray(a)
        arrays[f"in_{name}"] = a
        return nc.dram_tensor(f"in_{name}", a.shape, mybir.dt.from_np(a.dtype), kind="ExternalInput").ap()

    dense_t = dram("dense_t", np.asarray(inputs["dense_ctx"]).T)
    ids = dram("ids", inputs["ids"])
    last_ids = dram("last_ids", np.asarray(inputs["ids"])[:, N_FIELDS - N_PICKED:].T)
    tables = [dram(f"tbl_{f}", inputs[f"tbl_{f}"]) for f in range(N_FIELDS)]
    w1, w2 = dram("W_top1", inputs["W_top1"]), dram("W_top2", inputs["W_top2"])
    b1_t, b2_t, w3_t = (dram(n, np.asarray(inputs[n]).reshape(-1, P).T) for n in ("b_top1", "b_top2", "W_top3"))
    out = nc.dram_tensor("scores", (ids.shape[0], 1), F32, kind="ExternalOutput").ap()
    dlrm_tower(nc, dense_t, ids, last_ids, tables, w1, b1_t, w2, b2_t, w3_t, out)
    result = run_bass_kernel_spmd(nc, [arrays], core_ids=[0])
    return result.results[0]["scores"]
```
